# Optimizing a Trainium2 kernel written in Bass

```python
import numpy as np
import jax
import jax.numpy as jnp

def _softmax(x, axis=-1):
    return jax.nn.softmax(x, axis=axis)

def _gelu(x):
    return jax.nn.gelu(x, approximate=True)

def _silu(x):
    return jax.nn.silu(x)

def _sigmoid(x):
    return jax.nn.sigmoid(x)

def _layernorm(x, axis=-1, eps=1e-05):
    m = jnp.mean(x, axis=axis, keepdims=True)
    v = jnp.var(x, axis=axis, keepdims=True)
    return (x - m) / jnp.sqrt(v + eps)

def _scatter_add(tgt, idx, src, axis=0):
    return tgt.at[idx].add(src)

def _segment_sum(src, seg, n):
    return jax.ops.segment_sum(src, seg, n)
kernel_name = 'mk_adaln_ffn_d1_seqx_r2_4aee00'

def setup_inputs(seed: int=0):
    np.random.seed(seed)
    _w = jnp.asarray

    def _rec_inputs():
        import jax
        import jax.numpy as jnp
        _rk = jax.random.key(seed)
        x = -0.000125 + 0.9999 * jax.random.normal(jax.random.fold_in(_rk, 1), (4, 1024, 1024), jnp.float32)
        _lenS = 1024 - jax.random.randint(jax.random.fold_in(_rk, 7), (4,), 0, max(1, 1024 // 4) + 1, jnp.int32)
        _lenS2 = 1024 - jax.random.randint(jax.random.fold_in(_rk, 8), (4,), 0, max(1, 1024 // 4) + 1, jnp.int32)
        fside_BxSxS_0 = -1.52775e-05 + 0.999936 * jax.random.normal(jax.random.fold_in(_rk, 11), (4, 1024, 1024), jnp.float32)
        cond_512 = -5.03954e-05 + 1.00559 * jax.random.normal(jax.random.fold_in(_rk, 12), (4, 256), jnp.float32)
        return (x, fside_BxSxS_0, cond_512)
    x, fside_BxSxS_0, cond_512 = _rec_inputs()

    def _L0_cond_setup():
        import jax, jax.numpy as jnp
        from jax import lax
        import numpy as np
        B, T, C, TD = (8, 1024, 1024, 256)

        def _bi_wkv(r, k, v, w, u, time_emb):
            tf = jax.nn.sigmoid(jnp.sum(time_emb, axis=-1))[:, None, None]
            decay = jnp.exp(-jnp.exp(w.astype(jnp.float32)))[None, :] * (0.5 + 0.5 * tf[:, :, 0])
            kf = k.astype(jnp.float32)
            vf = v.astype(jnp.float32)
            ek = jnp.exp(jnp.minimum(kf, 30.0))
            ekv = ek * vf

            def step(carry, x):
                a, b = carry
                ekv_t, ek_t = x
                a = a * decay + ekv_t
                b = b * decay + ek_t
                return ((a, b), (a, b))
            ekv_t = jnp.swapaxes(ekv, 0, 1)
            ek_t = jnp.swapaxes(ek, 0, 1)
            init = (jnp.zeros_like(decay), jnp.zeros_like(decay))
            _, (nf, df) = lax.scan(step, init, (ekv_t, ek_t))
            _, (nb, db) = lax.scan(step, init, (ekv_t, ek_t), reverse=True)
            nf = jnp.swapaxes(nf, 0, 1)
            df = jnp.swapaxes(df, 0, 1)
            nb = jnp.swapaxes(nb, 0, 1)
            db = jnp.swapaxes(db, 0, 1)
            euk = jnp.exp(jnp.minimum(u.astype(jnp.float32)[None, None, :] + kf, 30.0))
            num = nf + nb - ekv + euk * vf
            den = df + db - ek + euk
            base = jax.nn.sigmoid(r.astype(jnp.float32)) * (num / jnp.maximum(den, 1e-08))
            out = base * (0.8 + 0.2 * tf)
            return out.astype(r.dtype)
        key = jax.random.key(seed)
        ks = jax.random.split(key, 6)
        return {'r': jax.random.normal(ks[0], (B, T, C), dtype=jnp.float32), 'k': jax.random.normal(ks[1], (B, T, C), dtype=jnp.float32), 'v': jax.random.normal(ks[2], (B, T, C), dtype=jnp.float32), 'w': jax.random.normal(ks[3], (C,), dtype=jnp.float32), 'u': jax.random.normal(ks[4], (C,), dtype=jnp.float32), 'time_emb': jax.random.normal(ks[5], (B, TD), dtype=jnp.float32)}
    _L0_cond_all = _L0_cond_setup()
    _L0_cond_in = {k: v for k, v in _L0_cond_all.items() if k in ('w', 'u')}
    del _L0_cond_all

    def _L0_ffn_setup():
        import jax, jax.numpy as jnp
        import numpy as np
        B, L, D = (4, 2048, 1024)
        DF = 4 * D
        CAPACITY_RATIO = 0.5
        key = jax.random.key(seed)
        ks = jax.random.split(key, 4)
        s = 0.02
        return {'x': jax.random.normal(ks[0], (B, L, D), dtype=jnp.float32), 'w_r': jax.random.normal(ks[1], (D,), dtype=jnp.float32) * s, 'b_r': jnp.zeros((), dtype=jnp.float32), 'w1': jax.random.normal(ks[2], (D, DF), dtype=jnp.float32) * s, 'b1': jnp.zeros((DF,), dtype=jnp.float32), 'w2': jax.random.normal(ks[3], (DF, D), dtype=jnp.float32) * s, 'b2': jnp.zeros((D,), dtype=jnp.float32)}
    _L0_ffn_all = _L0_ffn_setup()
    _L0_ffn_in = {k: v for k, v in _L0_ffn_all.items() if k in ('w_r', 'b_r', 'w1', 'b1', 'w2', 'b2')}
    del _L0_ffn_all
    return {'x': x, 'fside_BxSxS_0': fside_BxSxS_0, 'cond_512': cond_512, 'L0_cond_w': _L0_cond_in['w'], 'L0_cond_u': _L0_cond_in['u'], 'L0_ffn_w_r': _L0_ffn_in['w_r'], 'L0_ffn_b_r': _L0_ffn_in['b_r'], 'L0_ffn_w1': _L0_ffn_in['w1'], 'L0_ffn_b1': _L0_ffn_in['b1'], 'L0_ffn_w2': _L0_ffn_in['w2'], 'L0_ffn_b2': _L0_ffn_in['b2']}

def reference(x, fside_BxSxS_0, cond_512, L0_cond_w, L0_cond_u, L0_ffn_w_r, L0_ffn_b_r, L0_ffn_w1, L0_ffn_b1, L0_ffn_w2, L0_ffn_b2):
    import jax
    import jax.numpy as jnp

    def _L0_cond_ref(r, k, v, w, u, time_emb):
        import jax, jax.numpy as jnp
        from jax import lax
        import numpy as np
        B, T, C, TD = (8, 1024, 1024, 256)

        def _bi_wkv(r, k, v, w, u, time_emb):
            tf = jax.nn.sigmoid(jnp.sum(time_emb, axis=-1))[:, None, None]
            decay = jnp.exp(-jnp.exp(w.astype(jnp.float32)))[None, :] * (0.5 + 0.5 * tf[:, :, 0])
            kf = k.astype(jnp.float32)
            vf = v.astype(jnp.float32)
            ek = jnp.exp(jnp.minimum(kf, 30.0))
            ekv = ek * vf

            def step(carry, x):
                a, b = carry
                ekv_t, ek_t = x
                a = a * decay + ekv_t
                b = b * decay + ek_t
                return ((a, b), (a, b))
            ekv_t = jnp.swapaxes(ekv, 0, 1)
            ek_t = jnp.swapaxes(ek, 0, 1)
            init = (jnp.zeros_like(decay), jnp.zeros_like(decay))
            _, (nf, df) = lax.scan(step, init, (ekv_t, ek_t))
            _, (nb, db) = lax.scan(step, init, (ekv_t, ek_t), reverse=True)
            nf = jnp.swapaxes(nf, 0, 1)
            df = jnp.swapaxes(df, 0, 1)
            nb = jnp.swapaxes(nb, 0, 1)
            db = jnp.swapaxes(db, 0, 1)
            euk = jnp.exp(jnp.minimum(u.astype(jnp.float32)[None, None, :] + kf, 30.0))
            num = nf + nb - ekv + euk * vf
            den = df + db - ek + euk
            base = jax.nn.sigmoid(r.astype(jnp.float32)) * (num / jnp.maximum(den, 1e-08))
            out = base * (0.8 + 0.2 * tf)
            return out.astype(r.dtype)
        return _bi_wkv(r, k, v, w, u, time_emb)

    def _L0_ffn_ref(x, w_r, b_r, w1, b1, w2, b2):
        import jax, jax.numpy as jnp
        import numpy as np
        B, L, D = (4, 2048, 1024)
        DF = 4 * D
        CAPACITY_RATIO = 0.5
        b, l, d = x.shape
        k = int(l * CAPACITY_RATIO)
        scores = jnp.einsum('bld,d->bl', x, w_r) + b_r
        _, idx = jax.lax.top_k(scores, k)
        x_sel = jnp.take_along_axis(x, idx[:, :, None], axis=1)
        h = jax.nn.gelu(jnp.einsum('bkd,df->bkf', x_sel, w1) + b1)
        out_sel = jnp.einsum('bkf,fd->bkd', h, w2) + b2
        batch_ix = jnp.arange(b)[:, None]
        out = jnp.zeros_like(x).at[batch_ix, idx].set(out_sel)
        return out
    x = x + _L0_ffn_ref(_L0_cond_ref(x, fside_BxSxS_0, fside_BxSxS_0, L0_cond_w, L0_cond_u, cond_512), L0_ffn_w_r, L0_ffn_b_r, L0_ffn_w1, L0_ffn_b1, L0_ffn_w2, L0_ffn_b2)
    return x

_drawn_inputs = setup_inputs


def setup_inputs(seed=0):
    import zlib

    import numpy as np

    out = dict(_drawn_inputs(seed))
    spreads = {'L0_ffn_b1': (0.0, 0.1), 'L0_ffn_b2': (0.0, 0.1)}
    factors = {}
    for name, (base, spread) in spreads.items():
        noise = np.random.default_rng([zlib.crc32(name.encode()), seed]).standard_normal(out[name].shape)
        drawn = base * np.exp(spread * noise) if base else spread * noise
        out[name] = jnp.asarray(drawn.astype(out[name].dtype))
    for name, factor in factors.items():
        out[name] = (out[name] * factor).astype(out[name].dtype)
    return out
```

```python
import numpy as np
from contextlib import ExitStack

import concourse.bass as bass
from concourse import mybir

FP32 = mybir.dt.float32
FP32R = mybir.dt.float32r
FP16 = mybir.dt.float16
INT32 = mybir.dt.int32
UINT32 = mybir.dt.uint32
ALU = mybir.AluOpType
ACT = mybir.ActivationFunctionType
AXIS_X = mybir.AxisListType.X

P = 128
E30 = float(np.exp(np.float32(30.0)))
DEN_FLOOR = 1e-8

PERIOD = 6
FIRST = 1


def timetable(n_tiles, n_blocks):
    slots = [[] for _ in range(64)]
    for i in range(n_tiles):
        base = FIRST + PERIOD * i
        slots[base - 3 if i else 0].append(("load", i))
        slots[base] += [("keys", i), ("weigh", i)]
        if i:
            slots[base].append(("score_part", i - 1))
        slots[base + 1].append(("den_scans", i))
        slots[base + 2].append(("num_scans", i))
        slots[base + 3] += [("num_sum", i), ("den_back", i)]
        slots[base + 4] += [("num_back", i), ("divide_a", i)]
        slots[base + 5] += [("divide_b", i), ("keep", i)]
    end = FIRST + PERIOD * n_tiles
    slots[end] += [("score_part", n_tiles - 1), ("score", 0)]
    slots[end + 1] += [("score_rows", 0), ("rank_a", 0)]
    slots[end + 2] += [("rank_b", 0)]
    slots[end + 3] += [("one_hot", 0)]
    slots[end + 4] += [("choose", 0), ("fetch", 0)]
    for j in range(n_blocks):
        slots[56 + j].append(("take_rows", j))
    return slots


def prologue_steps(n_tiles, n_blocks):
    steps = [("load", 0), ("keys", 0)]
    for i in range(n_tiles):
        if i + 1 < n_tiles:
            steps.append(("load", i + 1))
        steps.append(("weigh", i))
        if i + 1 < n_tiles:
            steps.append(("keys", i + 1))
        steps.append(("den_scans", i))
        if i:
            steps.append(("score_part", i - 1))
        steps += [(s, i) for s in ("den_back", "num_scans", "num_sum", "num_back", "divide_a", "divide_b", "keep")]
    steps.append(("score_part", n_tiles - 1))
    steps += [(s, 0) for s in ("score", "score_rows", "rank_a", "rank_b", "one_hot", "choose", "fetch")]
    steps += [("take_rows", j) for j in range(n_blocks)]
    return steps


def wkv_ffn(nc, x, kv, cond, w, u, w_r, b_r, w1, b1, w2, b2, y_rows, out):
    B, T, C = x.shape
    F = w1.shape[1]
    K = T // 2
    NT, NC, NB = T // P, C // P, K // P
    LOT = 1024
    LT = LOT // P
    UNITS = 2 * LT * (F // LOT)
    assert (NT, NC, NB, LT, UNITS) == (8, 8, 4, 8, 64)
    TILES = B * NC
    RING = 4
    LEAD = RING - 1
    STEPS = timetable(NC, NB)
    PROLOGUE = prologue_steps(NC, NB)

    x_rows = x.rearrange("b t c -> (b t) c")
    out_rows = out.rearrange("b t c -> (b t) c")

    UNIT_CREDIT, HID_CREDIT, ACC_CREDIT, OUT_CREDIT = 1, 2, 2, 1

    with ExitStack() as ctx:
        def sb(name, shape, dtype=FP32):
            return ctx.enter_context(nc.sbuf_tensor(name, shape, dtype))

        def ps(name, shape):
            return ctx.enter_context(nc.psum_tensor(name, shape, FP32))

        def sem(name):
            return ctx.enter_context(nc.semaphore(name))

        w_raw = sb("w_raw", [P, 2, LT, 2 * P])
        w_hi = [sb(f"w_hi{k}", [P, LT, P], FP32R) for k in range(RING)]
        w_lo = [sb(f"w_lo{k}", [P, LT, P], FP32R) for k in range(RING)]
        x_hi = sb("x_hi", [P, NC, K], FP32R)
        x_lo = sb("x_lo", [P, NC, K], FP32R)
        h_hi = sb("h_hi", [P, LT, K], FP32R)
        h_lo = sb("h_lo", [P, LT, K], FP32R)
        h_raw = sb("h_raw", [P, 2, K])
        acc = sb("acc", [P, NC, K])
        x_row = sb("x_row", [P, NB, C])
        kv_in = sb("kv_in", [P, NT, P])
        x_in = sb("x_in", [P, NT, P])
        gate = sb("gate", [P, T])
        quad = sb("quad", [P, 4, T])
        ek, v, euk, ekv = (quad[:, k, :] for k in range(4))
        df = sb("df", [P, T])
        db = sb("db", [P, T])
        nf = sb("nf", [P, T])
        nb = sb("nb", [P, T])
        ry = sb("ry", [P, 2, T])
        rec, y = ry[:, 0, :], ry[:, 1, :]
        one_hot = ry[:, :, :].rearrange("p a t -> p (a t)").bitcast(FP16).rearrange("p (t k) -> p t k", k=K)
        ident = sb("ident", [P, P])
        before = sb("before", [P, P])
        iota_i = gate[:, 0:K].bitcast(INT32)
        tok_i = gate[:, K:K + NT].bitcast(INT32)
        slot_id = sb("slot_id", [P, K], FP16)
        tok_id = sb("tok_id", [P, NT], FP16)
        wr_row = sb("wr_row", [P, C])
        br_col = sb("br_col", [P, 1])
        NV = 3 * NC + F // P
        cond_all = nf[:, :].rearrange("p (b c) -> p b c", b=B)
        vec_rows = db[0:NV, 0:P]
        cols = sb("cols", [P, NV])
        w_col, u_col, b2_col, b1_col = cols[:, 0:NC], cols[:, NC:2 * NC], cols[:, 2 * NC:3 * NC], cols[:, 3 * NC:]
        dec_w = sb("dec_w", [P, NC])
        tf = sb("tf", [P, B])
        dec_f = sb("dec_f", [P, B])
        inv_c = sb("inv_c", [P, B])
        dec = sb("dec", [P, NC])
        inv_c_now = sb("inv_c_now", [P, 1])
        parts = sb("parts", [P, NT, NC])
        score = sb("score", [P, 2, NT])
        counts = sb("counts", [P, NT, 3])
        rank = sb("rank", [P, NT])
        row_base = sb("row_base", [P, 1])
        idx_y = sb("idx_y", [P, NB], UINT32)
        idx_next = sb("idx_next", [P, NB], UINT32)
        idx_now = sb("idx_now", [P, NB], UINT32)

        bank = [ps(f"bank{k}", [P, K]) for k in range(2)]
        kT = ps("kT", [P, T])
        denT = ps("denT", [P, T])
        numT = ps("numT", [P, T])
        chosen = numT[:, 0:NB]

        const_loaded = sem("const_loaded")
        const_pool = sem("const_pool")
        const_pe = sem("const_pe")
        const_act = sem("const_act")
        const_dve = sem("const_dve")
        raw_loaded = [sem(f"raw_loaded{k}") for k in range(2)]
        hi_split = sem("hi_split")
        lo_split = sem("lo_split")
        unit_done = sem("unit_done")
        gelu_done = sem("gelu_done")
        hid_hi_done = sem("hid_hi_done")
        hid_done = sem("hid_done")
        acc_init = sem("acc_init")
        acc_done = sem("acc_done")
        kv_loaded = sem("kv_loaded")
        x_loaded = sem("x_loaded")
        x_copied = sem("x_copied")
        keys_done = sem("keys_done")
        exp_done = sem("exp_done")
        gate_exp = sem("gate_exp")
        ek_done = sem("ek_done")
        ekv_done = sem("ekv_done")
        gate_done = sem("gate_done")
        decay_set = sem("decay_set")
        den_step = sem("den_step")
        den_done = sem("den_done")
        num_step = sem("num_step")
        num_done = sem("num_done")
        denT_done = sem("denT_done")
        numT_done = sem("numT_done")
        rec_step = sem("rec_step")
        y_done = sem("y_done")
        y_stored = sem("y_stored")
        yw_done = sem("yw_done")
        part_done = sem("part_done")
        score_step = sem("score_step")
        score_rows_done = sem("score_rows_done")
        count_step = sem("count_step")
        hot_step = sem("hot_step")
        chosen_done = sem("chosen_done")
        idx_step = sem("idx_step")
        idx_copied = sem("idx_copied")
        row_fetched = [sem(f"row_fetched{j}") for j in range(NB)]
        rowT_done = sem("rowT_done")
        x_hi_done = sem("x_hi_done")
        x_split = sem("x_split")
        x_row_loaded = [sem(f"x_row_loaded{j}") for j in range(NB)]
        outT_done = sem("outT_done")
        out_done = sem("out_done")
        scattered = sem("scattered")
        pool_passed = sem("pool_passed")

        def wait(eng, semaphore, count):
            if not (isinstance(count, int) and count <= 0):
                eng.wait_ge(semaphore, count)

        def known(eng, count):
            return count if isinstance(count, int) else eng.snap(count)

        RANK_OPS = 3 * NT - 1

        block = ctx.enter_context(nc.Block())

        @block.sync
        def _(sp):
            for k, vec in enumerate((w, u, b2)):
                sp.dma_start(vec_rows[k * NC:(k + 1) * NC, :], vec.rearrange("(t p) -> t p", p=P)).then_inc(const_loaded, 16)
            sp.dma_start(vec_rows[3 * NC:NV, :], b1.rearrange("(t p) -> t p", p=P)).then_inc(const_loaded, 16)
            sp.dma_start(cond_all, cond.partition_broadcast(P)).then_inc(const_loaded, 16)
            sp.dma_start(wr_row[:], w_r.partition_broadcast(P)).then_inc(const_loaded, 16)
            sp.dma_start(br_col[:], b_r.partition_broadcast(P)).then_inc(const_loaded, 16)

            def met():
                sp.wait_ge(const_loaded, 16 * 7)

            def load_weights(b, pair):
                lot, r = divmod(2 * pair, 2 * LT)
                if r < LT:
                    src = w1[:, lot * LOT + r * P:lot * LOT + (r + 2) * P]
                else:
                    src = w2[lot * LOT:(lot + 1) * LOT, (r - LT) * P:(r - LT + 2) * P]
                wait(sp, lo_split, UNITS * b + 2 * pair - 2)
                sp.dma_start(w_raw[:, pair % 2], src.rearrange("(k p) n -> p k n", p=P)).then_inc(raw_loaded[pair % 2], 16)

            def front_step(step, i, fb):
                n = NC * fb + i
                cs = slice(i * P, (i + 1) * P)
                if step == "load":
                    kv_src = kv_b(fb)[:, :, cs]
                    x_src = x_b(fb)[:, :, cs]
                    n, n_copied = known(sp, n), known(sp, 16 * n)
                    met()
                    wait(sp, keys_done, n)
                    sp.dma_start(kv_in[:], kv_src).then_inc(kv_loaded, 16)
                    met()
                    wait(sp, gate_exp, n)
                    wait(sp, x_copied, n_copied)
                    sp.dma_start(x_in[:], x_src).then_inc(x_loaded, 16)
                elif step == "keep":
                    y_dst = y_rows.rearrange("(t p) c -> p t c", p=P)[:, :, cs]
                    if i == 0:
                        for j in range(NB):
                            wait(sp, row_fetched[j], 16 * fb)
                    met()
                    sp.wait_ge(y_done, n + 1)
                    sp.dma_start(y_dst, y.rearrange("p (t c) -> p t c", c=P)).then_inc(y_stored, 16)

            def of_batch(rows, fb):
                start = fb * T if isinstance(fb, int) else sp.snap(fb * T)
                return rows[bass.ds(start, T), :].rearrange("(t p) c -> p t c", p=P)

            def kv_b(fb):
                return of_batch(kv.rearrange("b t c -> (b t) c"), fb)

            def x_b(fb):
                return of_batch(x_rows, fb)

            for k, (step, i) in enumerate(PROLOGUE):
                front_step(step, i, 0)
                if (step, i) == ("load", 1):
                    load_weights(0, 0)
                    load_weights(0, 1)
            load_weights(0, 2)

            def batch(b, front):
                for s in range(UNITS):
                    if s % 2 == 0 and (front or s // 2 + 3 < UNITS // 2):
                        pair = s // 2 + 3
                        if pair < UNITS // 2:
                            load_weights(b, pair)
                        else:
                            load_weights(b + 1, pair - UNITS // 2)
                    if front:
                        for step, i in STEPS[s]:
                            front_step(step, i, b + 1)

            with sp.Fori(0, B - 1) as b:
                batch(b, True)
            batch(B - 1, False)
            sp.wait_ge(scattered, 16 * NB * B)
            sp.wait_ge(x_copied, 16 * TILES)
            sp.wait_ge(y_stored, 16 * TILES)

        @block.tensor
        def _(pe):
            pe.sem_inc(unit_done, UNIT_CREDIT)
            pe.sem_inc(outT_done, OUT_CREDIT)
            pe.wait_ge(const_loaded, 16 * 7)
            pe.wait_ge(const_pool, 2)
            nc.tensor.transpose(kT[:, 0:NV], vec_rows, ident[0:NV, 0:NV]).then_inc(const_pe, 1)

            def turn(dst, src, count, ready):
                for k in range(count):
                    last = nc.tensor.transpose(dst[:, k * P:(k + 1) * P], src(k), ident[:])
                last.then_inc(ready, 1)

            def front_step(step, i, fb):
                n = NC * fb + i
                if step == "keys":
                    pe.wait_ge(kv_loaded, 16 * (n + 1))
                    wait(pe, exp_done, 3 * n)
                    if i == 0 and not isinstance(fb, int):
                        pe.wait_ge(out_done, OUT_CREDIT + NB * (fb - 1))
                    if isinstance(n, int) and n == 0:
                        pe.wait_ge(const_dve, 1)
                    turn(kT, lambda k: kv_in[:, k, :], NT, keys_done)
                elif step == "den_back":
                    pe.wait_ge(den_done, n + 1)
                    turn(denT, lambda k: df[:, k * P:(k + 1) * P], NT, denT_done)
                elif step == "num_back":
                    pe.wait_ge(num_done, n + 1)
                    turn(numT, lambda k: nf[:, k * P:(k + 1) * P], NT, numT_done)
                elif step == "score_rows":
                    pe.wait_ge(score_step, 3 * fb + 3)
                    turn(denT, lambda k: nf[:, k * P:(k + 1) * P], NT, score_rows_done)
                elif step == "choose":
                    pe.wait_ge(hot_step, 9 * fb + 9)
                    for j in range(NB):
                        for t in range(NT):
                            last = nc.tensor.matmul(chosen[:, j:j + 1], one_hot[:, t, j * P:(j + 1) * P],
                                                    tok_id[:, t:t + 1], start=(t == 0), stop=(t == NT - 1))
                    last.then_inc(chosen_done, 1)
                elif step == "take_rows":
                    pe.wait_ge(row_fetched[i], 16 * (fb + 1))
                    if i == 0:
                        pe.wait_ge(exp_done, 3 * NC * (fb + 1))
                    elif i == 1:
                        pe.wait_ge(idx_step, 3 * fb + 2)
                    else:
                        pe.wait_ge(x_split, NB * fb + i - 1)
                    turn(kT if i % 2 == 0 else numT, lambda k: quad[:, i, k * P:(k + 1) * P], NC, rowT_done)

            for step, i in PROLOGUE:
                front_step(step, i, 0)

            def unit(b, s):
                lot, r = divmod(s, 2 * LT)
                hidden = LT * (F // LOT) * b + LT * lot
                k_hi, k_lo = w_hi[s % RING], w_lo[s % RING]
                if r < 2:
                    pe.wait_ge(acc_done, ACC_CREDIT + hidden - 1 + r)
                elif r < LT + 2:
                    pe.wait_ge(gelu_done, hidden + r - 1)
                else:
                    pe.wait_ge(acc_done, ACC_CREDIT + hidden + r - LT - 1)
                if s == 0:
                    pe.wait_ge(x_split, NB * (b + 1))
                pe.wait_ge(lo_split, UNITS * b + s + 1)
                m_hi, m_lo = (x_hi, x_lo) if r < LT else (h_hi, h_lo)
                for k in range(LT):
                    if r == LT:
                        pe.wait_ge(hid_done, HID_CREDIT + hidden + k + 1)
                    nc.tensor.matmul(bank[s % 2][:], k_hi[:, k, :], m_hi[:, k, :], start=(k == 0), stop=False)
                    nc.tensor.matmul(bank[s % 2][:], k_hi[:, k, :], m_lo[:, k, :], start=False, stop=False)
                    last = nc.tensor.matmul(bank[s % 2][:], k_lo[:, k, :], m_hi[:, k, :], start=False, stop=(k == LT - 1))
                last.then_inc(unit_done, 1)

            def output_back(b, front):
                pe.wait_ge(acc_done, ACC_CREDIT + LT * (F // LOT) * (b + 1))
                if front:
                    pe.wait_ge(x_split, NB * (b + 2))
                for j in range(NB):
                    if j == 3:
                        pe.wait_ge(out_done, OUT_CREDIT + NB * b + 1)
                    turn((denT, kT, numT, denT)[j], lambda k: acc[:, k, j * P:(j + 1) * P], NC, outT_done)

            def batch(b, front):
                for s in range(UNITS):
                    unit(b, s)
                    if front:
                        for step, i in STEPS[s]:
                            front_step(step, i, b + 1)
                output_back(b, front)

            with pe.Fori(0, B - 1) as b:
                batch(b, True)
            batch(B - 1, False)

        @block.scalar
        def _(act):
            act.wait_ge(const_dve, 1)
            nc.scalar.activation(dec_w[:], w_col, ACT.Exp).then_inc(const_act, 1)
            act.wait_ge(const_act, 1)
            nc.scalar.activation(dec_w[:], dec_w[:], ACT.Exp, scale=-1.0).then_inc(const_act, 1)
            act.wait_ge(const_dve, 2)
            nc.scalar.activation(tf[:], tf[:], ACT.Exp, scale=-1.0).then_inc(const_act, 1)

            def split_hi(b, s):
                pair = s // 2
                wait(act, unit_done, UNIT_CREDIT + UNITS * b + s - LEAD)
                act.wait_ge(raw_loaded[pair % 2], 16 * (UNITS // 4 * b + pair // 2 + 1))
                nc.scalar.activation(w_hi[s % RING][:], w_raw[:, pair % 2, :, (s % 2) * P:(s % 2 + 1) * P],
                                     ACT.Copy).then_inc(hi_split, 1)

            def front_step(step, i, fb):
                n = NC * fb + i
                if step == "weigh":
                    act.wait_ge(keys_done, n + 1)
                    wait(act, num_done, n)
                    if i == 0:
                        wait(act, rowT_done, NB * fb)
                    nc.scalar.activation(ek, kT[:], ACT.Exp).then_inc(exp_done, 1)
                    nc.scalar.activation(v, kT[:], ACT.Copy).then_inc(exp_done, 1)
                    nc.scalar.activation(euk, kT[:], ACT.Exp, bias=u_col[:, i:i + 1]).then_inc(exp_done, 1)
                    x_dst = out_rows[bass.ds(fb * T, T), i * P:(i + 1) * P].rearrange("(t p) c -> p t c", p=P)
                    act.wait_ge(x_loaded, 16 * (n + 1))
                    act.dma_start(x_dst, x_in[:]).then_inc(x_copied, 16)
                    wait(act, y_done, n)
                    if isinstance(n, int) and n == 0:
                        act.wait_ge(const_dve, 13)
                    nc.scalar.activation(gate[:], x_in[:].rearrange("p t c -> p (t c)"), ACT.Exp,
                                         scale=-1.0).then_inc(gate_exp, 1)
                elif step == "take_rows":
                    act.wait_ge(rowT_done, NB * fb + i + 1)
                    src = kT if i % 2 == 0 else numT
                    nc.scalar.activation(x_hi[:, :, i * P:(i + 1) * P], src[:].rearrange("p (c r) -> p c r", r=P),
                                         ACT.Copy).then_inc(x_hi_done, 1)

            for step, i in PROLOGUE:
                front_step(step, i, 0)
                if (step, i) == ("weigh", 2):
                    for s in range(LEAD):
                        split_hi(0, s)

            def batch(b, front):
                for s in range(UNITS):
                    lot, r = divmod(s, 2 * LT)
                    if s + LEAD < UNITS:
                        split_hi(b, s + LEAD)
                    elif front:
                        split_hi(b + 1, s + LEAD - UNITS)
                    if r < LT:
                        m = LT * (F // LOT) * b + LT * lot + r
                        act.wait_ge(unit_done, UNIT_CREDIT + UNITS * b + s + 1)
                        act.wait_ge(hid_done, HID_CREDIT + m - 1)
                        nc.scalar.activation(h_raw[:, r % 2, :], bank[s % 2][:], ACT.Gelu_apprx_tanh,
                                             bias=b1_col[:, LT * lot + r:LT * lot + r + 1]).then_inc(gelu_done, 1)
                    if front:
                        for step, i in STEPS[s]:
                            front_step(step, i, b + 1)

            with act.Fori(0, B - 1) as b:
                batch(b, True)
            batch(B - 1, False)

        @block.vector
        def _(dve):
            dve.sem_inc(hid_done, HID_CREDIT)
            dve.sem_inc(acc_done, ACC_CREDIT)
            dve.sem_inc(out_done, OUT_CREDIT)
            dve.wait_ge(const_pe, 1)
            nc.vector.tensor_copy(cols[:], kT[:, 0:NV]).then_inc(const_dve, 1)
            nc.vector.tensor_reduce(tf[:], cond_all, AXIS_X, ALU.add).then_inc(const_dve, 1)
            dve.wait_ge(const_act, 3)
            nc.vector.tensor_scalar(tf[:], tf[:], 1.0, None, ALU.add).then_inc(const_dve, 1)
            dve.wait_ge(const_dve, 3)
            nc.vector.reciprocal(tf[:], tf[:]).then_inc(const_dve, 1)
            dve.wait_ge(const_dve, 4)
            nc.vector.tensor_scalar(dec_f[:], tf[:], 0.5, 0.5, ALU.mult, ALU.add).then_inc(const_dve, 1)
            nc.vector.tensor_scalar(inv_c[:], tf[:], 0.2, 0.8, ALU.mult, ALU.add).then_inc(const_dve, 1)
            dve.wait_ge(const_dve, 6)
            nc.vector.reciprocal(inv_c[:], inv_c[:]).then_inc(const_dve, 1)
            nc.vector.memset(db[:, T - 1:T], 0.0).then_inc(const_dve, 1)
            nc.vector.memset(nb[:, T - 1:T], 0.0).then_inc(const_dve, 1)
            nc.vector.memset(counts[:], 0.0).then_inc(const_dve, 1)
            nc.vector.memset(row_base[:], 0.0).then_inc(const_dve, 1)
            dve.wait_ge(const_pool, 5)
            nc.vector.tensor_copy(slot_id[:], iota_i).then_inc(const_dve, 1)
            nc.vector.tensor_copy(tok_id[:], tok_i).then_inc(const_dve, 1)
            dve.wait_ge(const_dve, 13)

            def count(out, in0, scalar, op, t):
                nc.vector.tensor_scalar(out, in0, scalar, 0.0, op, ALU.add, accum_out=t).then_inc(count_step, 1)

            def rank_tiles(fb, tiles):
                done = RANK_OPS * fb + (3 * tiles[0] - 1 if tiles[0] else 0)
                for t in tiles:
                    col = score[:, 1, t:t + 1]
                    if t:
                        wait(dve, count_step, done)
                        count(df[:, 0:t * P], denT[:, 0:t * P], col, ALU.is_ge, counts[:, t, 0:1])
                        done = done + 1
                    wait(dve, count_step, done)
                    count(df[:, t * P:T], denT[:, t * P:T], col, ALU.is_gt, counts[:, t, 1:2])
                    done = done + 1
                    dve.wait_ge(count_step, done)
                    nc.vector.scalar_tensor_tensor(df[:, t * P:(t + 1) * P], denT[:, t * P:(t + 1) * P], col, before[:],
                                                   ALU.is_equal, ALU.mult, accum_out=counts[:, t, 2:3]).then_inc(count_step, 1)
                    done = done + 1

            def front_step(step, i, fb):
                n = NC * fb + i
                if step == "den_scans":
                    if i == 0:
                        nc.vector.tensor_scalar(dec[:], dec_w[:], dec_f[:, bass.ds(fb, 1)], None,
                                                ALU.mult).then_inc(decay_set, 1)
                        nc.vector.tensor_scalar(inv_c_now[:], inv_c[:, bass.ds(fb, 1)], 1.0, None,
                                                ALU.mult).then_inc(decay_set, 1)
                    decay = dec[:, i:i + 1].to_broadcast([P, T])
                    dve.wait_ge(decay_set, 2 * fb + 2)
                    dve.wait_ge(ek_done, n + 1)
                    wait(dve, denT_done, n)
                    nc.vector.tensor_tensor_scan(df[:], decay, ek, 0.0, ALU.mult, ALU.add).then_inc(den_step, 1)
                    nc.vector.tensor_tensor_scan(db[:, T - 2::-1], ek[:, T - 1:0:-1], decay[:, 0:T - 1], 0.0,
                                                 ALU.add, ALU.mult).then_inc(den_step, 1)
                    dve.wait_ge(den_step, 3 * n + 1)
                    dve.wait_ge(exp_done, 3 * n + 3)
                    nc.vector.scalar_tensor_tensor(df[:], euk, E30, df[:], ALU.min, ALU.add).then_inc(den_step, 1)
                    dve.wait_ge(den_step, 3 * n + 3)
                    nc.vector.tensor_tensor(df[:], df[:], db[:], ALU.add).then_inc(den_done, 1)
                elif step == "num_scans":
                    decay = dec[:, i:i + 1].to_broadcast([P, T])
                    dve.wait_ge(ekv_done, n + 1)
                    wait(dve, numT_done, n)
                    nc.vector.tensor_tensor_scan(nf[:], decay, ekv, 0.0, ALU.mult, ALU.add).then_inc(num_step, 1)
                    nc.vector.tensor_tensor_scan(nb[:, T - 2::-1], ekv[:, T - 1:0:-1], decay[:, 0:T - 1], 0.0,
                                                 ALU.add, ALU.mult).then_inc(num_step, 1)
                    nc.vector.scalar_tensor_tensor(euk, euk, E30, v, ALU.min, ALU.mult).then_inc(num_step, 1)
                elif step == "num_sum":
                    dve.wait_ge(num_step, 4 * n + 2)
                    nc.vector.tensor_tensor(nf[:], nf[:], nb[:], ALU.add).then_inc(num_step, 1)
                    dve.wait_ge(num_step, 4 * n + 4)
                    nc.vector.tensor_tensor(nf[:], nf[:], euk, ALU.add).then_inc(num_done, 1)
                elif step == "divide_a":
                    dve.wait_ge(denT_done, n + 1)
                    dve.wait_ge(gate_done, n + 1)
                    nc.vector.scalar_tensor_tensor(rec, denT[:], DEN_FLOOR, gate[:], ALU.max,
                                                   ALU.mult).then_inc(rec_step, 1)
                    dve.wait_ge(rec_step, 3 * n + 1)
                    nc.vector.reciprocal(rec[:, 0:T // 2], rec[:, 0:T // 2]).then_inc(rec_step, 1)
                elif step == "divide_b":
                    nc.vector.reciprocal(rec[:, T // 2:], rec[:, T // 2:]).then_inc(rec_step, 1)
                    dve.wait_ge(rec_step, 3 * n + 3)
                    dve.wait_ge(numT_done, n + 1)
                    wait(dve, y_stored, 16 * n)
                    wait(dve, yw_done, n)
                    if i == 0:
                        wait(dve, chosen_done, fb)
                    nc.vector.tensor_tensor(y, numT[:], rec, ALU.mult).then_inc(y_done, 1)
                elif step == "score_part":
                    dve.wait_ge(yw_done, n + 1)
                    nc.vector.tensor_reduce(parts[:, :, i], rec.rearrange("p (t c) -> p t c", c=P), AXIS_X,
                                            ALU.add).then_inc(part_done, 1)
                elif step == "score":
                    dve.wait_ge(part_done, NC * (fb + 1))
                    nc.vector.tensor_reduce(score[:, 0, :], parts[:], AXIS_X, ALU.add).then_inc(score_step, 1)
                    dve.wait_ge(score_step, 3 * fb + 1)
                    nc.vector.tensor_scalar(score[:, 1, :], score[:, 0, :], br_col[:, 0:1], None,
                                            ALU.add).then_inc(score_step, 1)
                    dve.wait_ge(score_step, 3 * fb + 2)
                    dve.wait_ge(numT_done, NC * (fb + 1))
                    nc.vector.tensor_copy(nf[:].rearrange("p (t c) -> p t c", c=P),
                                          score[:, 1, :].unsqueeze(2).to_broadcast([P, NT, P])).then_inc(score_step, 1)
                elif step == "rank_a":
                    dve.wait_ge(score_rows_done, fb + 1)
                    rank_tiles(fb, range(0, NT // 2))
                elif step == "rank_b":
                    rank_tiles(fb, range(NT // 2, NT))
                elif step == "one_hot":
                    dve.wait_ge(count_step, RANK_OPS * (fb + 1))
                    nc.vector.tensor_reduce(rank[:], counts[:], AXIS_X, ALU.add).then_inc(hot_step, 1)
                    dve.wait_ge(hot_step, 9 * fb + 1)
                    dve.wait_ge(y_stored, 16 * NC * (fb + 1))
                    for t in range(NT):
                        nc.vector.tensor_scalar(one_hot[:, t, :], slot_id[:], rank[:, t:t + 1], None,
                                                ALU.is_equal).then_inc(hot_step, 1)
                elif step == "choose":
                    dve.wait_ge(chosen_done, fb + 1)
                    wait(dve, idx_copied, fb)
                    nc.vector.tensor_copy(idx_y[:], chosen).then_inc(idx_step, 1)
                    nc.vector.tensor_scalar(idx_next[:], chosen, row_base[:, 0:1], None, ALU.add).then_inc(idx_step, 1)
                    dve.wait_ge(idx_step, 3 * fb + 2)
                    nc.vector.tensor_scalar(row_base[:], row_base[:], float(T), None, ALU.add).then_inc(idx_step, 1)
                elif step == "take_rows":
                    dve.wait_ge(x_hi_done, NB * fb + i + 1)
                    src = kT if i % 2 == 0 else numT
                    rows = slice(i * P, (i + 1) * P)
                    nc.vector.tensor_tensor(x_lo[:, :, rows], src[:].rearrange("p (c r) -> p c r", r=P),
                                            x_hi[:, :, rows].bitcast(FP32), ALU.subtract).then_inc(x_split, 1)

            for step, i in PROLOGUE:
                front_step(step, i, 0)

            def batch(b, front):
                for s in range(UNITS):
                    lot, r = divmod(s, 2 * LT)
                    if r < LT:
                        m = LT * (F // LOT) * b + LT * lot + r
                        dve.wait_ge(gelu_done, m + 1)
                        nc.vector.tensor_copy(h_hi[:, r, :], h_raw[:, r % 2, :]).then_inc(hid_hi_done, 1)
                        dve.wait_ge(hid_hi_done, m + 1)
                        nc.vector.tensor_tensor(h_lo[:, r, :], h_raw[:, r % 2, :], h_hi[:, r, :].bitcast(FP32),
                                                ALU.subtract).then_inc(hid_done, 1)
                    else:
                        dve.wait_ge(unit_done, UNIT_CREDIT + UNITS * b + s + 1)
                        if s == LT:
                            dve.wait_ge(acc_init, b + 1)
                        nc.vector.tensor_tensor(acc[:, r - LT, :], acc[:, r - LT, :], bank[s % 2][:],
                                                ALU.add).then_inc(acc_done, 1)
                    if front:
                        for step, i in STEPS[s]:
                            front_step(step, i, b + 1)
                for j in range(NB):
                    dve.wait_ge(outT_done, OUT_CREDIT + NB * b + j + 1)
                    dve.wait_ge(x_row_loaded[j], 16 * (b + 1))
                    nc.vector.tensor_tensor(x_row[:, j, :], (denT, kT, numT, denT)[j][:], x_row[:, j, :],
                                            ALU.add).then_inc(out_done, 1)

            with dve.Fori(0, B - 1) as b:
                batch(b, True)
            batch(B - 1, False)

        @block.gpsimd
        def _(pool):
            nc.gpsimd.memset(ident[:], 0.0).then_inc(const_pool, 1)
            pool.wait_ge(const_pool, 1)
            nc.gpsimd.affine_select(out=ident[:], in_=ident[:], compare_op=ALU.not_equal, fill=1.0, base=0,
                                    pattern=[[-1, P]], channel_multiplier=1).then_inc(const_pool, 1)
            nc.gpsimd.memset(before[:], 1.0).then_inc(const_pool, 1)
            nc.gpsimd.iota(iota_i, pattern=[[1, K]], base=0, channel_multiplier=0).then_inc(const_pool, 1)
            nc.gpsimd.iota(tok_i, pattern=[[P, NT]], base=0, channel_multiplier=1).then_inc(const_pool, 1)
            pool.wait_ge(const_pool, 3)
            nc.gpsimd.affine_select(out=before[:], in_=before[:], compare_op=ALU.is_gt, fill=0.0, base=0,
                                    pattern=[[-1, P]], channel_multiplier=1).then_inc(const_pool, 1)

            def passed():
                pool.sem_inc(pool_passed, 1)

            def split_lo(b, s):
                pair = s // 2
                pool.wait_ge(hi_split, UNITS * b + s + 1)
                nc.gpsimd.tensor_tensor(w_lo[s % RING][:], w_raw[:, pair % 2, :, (s % 2) * P:(s % 2 + 1) * P],
                                        w_hi[s % RING][:].bitcast(FP32), ALU.subtract).then_inc(lo_split, 1)

            def front_step(step, i, fb):
                n = NC * fb + i
                if step == "weigh":
                    pool.wait_ge(exp_done, 3 * n + 1)
                    passed()
                    nc.gpsimd.tensor_scalar(ek, ek, E30, 0.0, ALU.min, ALU.max).then_inc(ek_done, 1)
                    pool.wait_ge(ek_done, n + 1)
                    pool.wait_ge(exp_done, 3 * n + 2)
                    nc.gpsimd.tensor_tensor(ekv, ek, v, ALU.mult).then_inc(ekv_done, 1)
                    pool.wait_ge(gate_exp, n + 1)
                    pool.wait_ge(decay_set, 2 * fb + 2)
                    passed()
                    nc.gpsimd.tensor_scalar(gate[:], gate[:], inv_c_now[:, 0:1], inv_c_now[:, 0:1], ALU.mult,
                                            ALU.add).then_inc(gate_done, 1)
                elif step == "keep":
                    pool.wait_ge(y_done, n + 1)
                    nc.gpsimd.tensor_tensor(rec.rearrange("p (t c) -> p t c", c=P), y.rearrange("p (t c) -> p t c", c=P),
                                            wr_row[:, i * P:(i + 1) * P].unsqueeze(1).to_broadcast([P, NT, P]),
                                            ALU.mult).then_inc(yw_done, 1)
                elif step == "fetch":
                    pool.wait_ge(idx_step, 3 * fb + 2)
                    pool.wait_ge(y_stored, 16 * NC * (fb + 1))
                    pool.wait_ge(num_done, NC * (fb + 1))
                    passed()
                    for j in range(NB):
                        nc.gpsimd.indirect_dma_start(
                            out=quad[:, j, :], out_offset=None, in_=y_rows,
                            in_offset=bass.IndirectOffsetOnAxis(ap=idx_y[:, j:j + 1], axis=0),
                        ).then_inc(row_fetched[j], 16)

            def fetch_x_rows(fb):
                wait(pool, scattered, 16 * NB * fb)
                pool.wait_ge(idx_step, 3 * fb + 2)
                passed()
                nc.gpsimd.tensor_copy(idx_now[:], idx_next[:]).then_inc(idx_copied, 1)
                pool.wait_ge(idx_copied, fb + 1)
                passed()
                for j in range(NB):
                    nc.gpsimd.indirect_dma_start(
                        out=x_row[:, j, :], out_offset=None, in_=x_rows,
                        in_offset=bass.IndirectOffsetOnAxis(ap=idx_now[:, j:j + 1], axis=0),
                    ).then_inc(x_row_loaded[j], 16)

            def store_rows(b):
                for j in range(NB):
                    pool.wait_ge(out_done, OUT_CREDIT + NB * b + j + 1)
                    pool.wait_ge(x_copied, 16 * NC * (b + 1))
                    passed()
                    nc.gpsimd.indirect_dma_start(
                        out=out_rows, out_offset=bass.IndirectOffsetOnAxis(ap=idx_now[:, j:j + 1], axis=0),
                        in_=x_row[:, j, :], in_offset=None,
                    ).then_inc(scattered, 16)

            pool.wait_ge(const_dve, 1)
            pool.wait_ge(const_dve, 13)
            for step, i in PROLOGUE:
                front_step(step, i, 0)
                if (step, i) == ("weigh", 2):
                    for s in range(LEAD):
                        split_lo(0, s)
            fetch_x_rows(0)

            def batch(b, front):
                for s in range(UNITS):
                    if s + LEAD < UNITS:
                        split_lo(b, s + LEAD)
                    elif front:
                        split_lo(b + 1, s + LEAD - UNITS)
                    if s == 3:
                        pool.wait_ge(outT_done, OUT_CREDIT + NB * b)
                        passed()
                        nc.gpsimd.tensor_copy(acc[:], b2_col.unsqueeze(2).to_broadcast([P, NC, K])).then_inc(acc_init, 1)
                    if front:
                        for step, i in STEPS[s]:
                            front_step(step, i, b + 1)
                store_rows(b)
                if front:
                    fetch_x_rows(b + 1)

            with pool.Fori(0, B - 1) as b:
                batch(b, True)
            batch(B - 1, False)


_INS = ["x", "fside_BxSxS_0", "cond_512", "L0_cond_w", "L0_cond_u", "L0_ffn_w_r", "L0_ffn_b_r",
        "L0_ffn_w1", "L0_ffn_b1", "L0_ffn_w2", "L0_ffn_b2"]


def kernel(**inputs):
    import numpy as _np
    import concourse.bacc as _bacc
    from concourse import mybir as _mybir
    from concourse.bass_utils import run_bass_kernel_spmd as _run

    nc = _bacc.Bacc("TRN2", target_bir_lowering=False, num_devices=1, dynamic_dma_scratch_size=4096)
    arrays, args = {}, []
    for name in _INS:
        a = _np.ascontiguousarray(inputs[name])
        if a.ndim == 0:
            a = a.reshape(1)
        arrays[f"in_{name}"] = a
        args.append(nc.dram_tensor(f"in_{name}", a.shape, _mybir.dt.from_np(a.dtype), kind="ExternalInput").ap())
    B, T, C = arrays["in_x"].shape
    y_rows = nc.dram_tensor("y_rows", (T, C), _mybir.dt.float32).ap()
    out = nc.dram_tensor("out_x", (B, T, C), _mybir.dt.float32, kind="ExternalOutput").ap()
    wkv_ffn(nc, *args, y_rows, out)
    r = _run(nc, [arrays], core_ids=[0])
    return r.results[0]["out_x"]
```

```python
import numpy as np
from contextlib import ExitStack

import concourse.bass as bass
from concourse import mybir

FP32 = mybir.dt.float32
FP32R = mybir.dt.float32r
FP16 = mybir.dt.float16
INT32 = mybir.dt.int32
UINT32 = mybir.dt.uint32
ALU = mybir.AluOpType
ACT = mybir.ActivationFunctionType
AXIS_X = mybir.AxisListType.X

P = 128
E30 = float(np.exp(np.float32(30.0)))
DEN_FLOOR = 1e-8

LOT = 1024
UNITS = 64
PERIOD = 6
FIRST = 1


class FrontBuffers:

    def __init__(self, kv_in, x_in, gate, quad, sums, rec, y):
        self.kv_in, self.x_in, self.gate = kv_in, x_in, gate
        self.ek, self.v, self.euk, self.ekv = (quad[:, k, :] for k in range(4))
        self.df, self.db, self.nf, self.nb = (sums[:, k, :] for k in range(4))
        self.rec, self.y = rec, y


def timetable(n_tiles, n_blocks):
    slots = [[] for _ in range(UNITS)]
    for i in range(n_tiles):
        base = FIRST + PERIOD * i
        if i:
            slots[base - 3] += [("load_kv", i), ("load_x", i)]
        slots[base] += [("keys", i), ("weigh", i)]
        slots[base + 1] += [("clamp", i), ("den_scans", i)]
        slots[base + 2] += [("gate", i), ("den_sum", i), ("num_scans", i)]
        slots[base + 3] += [("divide_a", i), ("own_part", i)]
        slots[base + 4] += [("divide_b", i), ("num_sum", i)]
        slots[base + 5] += [("quotient", i)]
        if i:
            slots[base + 5].append(("score_part", i - 1))
        slots[base + 7] += [("num_back", i), ("weight", i), ("keep", i)]
    end = FIRST + PERIOD * n_tiles
    slots[end + 2] += [("score_part", n_tiles - 1), ("score", 0)]
    slots[end + 3] += [("score_rows", 0), ("rank_a", 0)]
    slots[end + 4] += [("rank_b", 0)]
    slots[end + 5] += [("one_hot", 0)]
    slots[end + 7] += [("choose", 0), ("fetch", 0)]
    for j in range(n_blocks):
        slots[end + 9 + j].append(("take_rows", j))
    return slots


def prologue_steps(n_tiles, n_blocks):
    steps = [("load_kv", 0), ("load_x", 0), ("load_kv", 1), ("load_x", 1), ("keys", 0), ("weigh", 0),
             ("gate", 0), ("clamp", 0)]
    for i in range(n_tiles + 1):
        more = i + 1 < n_tiles
        if more:
            steps.append(("keys", i + 1))
        if i + 2 < n_tiles:
            steps.append(("load_kv", i + 2))
        if i:
            steps += [("num_back", i - 1), ("divide_a", i - 1), ("seed", i - 1)]
            if more:
                steps.append(("load_x", i + 1))
        if i < n_tiles:
            steps += [("den_scans", i), ("den_back", i), ("num_scans", i)]
        if more:
            steps += [("weigh", i + 1), ("gate", i + 1), ("clamp", i + 1)]
        if i:
            steps += [("divide_b", i - 1), ("weight", i - 1), ("keep", i - 1)]
        if i > 1:
            steps.append(("score_part", i - 2))
    steps.append(("score_part", n_tiles - 1))
    steps += [(s, 0) for s in ("score", "score_rows", "rank_a", "rank_b", "one_hot", "choose", "fetch")]
    steps += [("take_rows", j) for j in range(n_blocks)]
    return steps


def wkv_ffn(nc, x, kv, cond, w, u, w_r, b_r, w1, b1, w2, b2, y_rows, out):
    B, T, C = x.shape
    F = w1.shape[1]
    K = T // 2
    NT, NC, NB = T // P, C // P, K // P
    LT = LOT // P
    assert (NT, NC, NB, LT) == (8, 8, 4, 8) and UNITS == 2 * LT * (F // LOT)
    TILES = B * NC
    RING = 4
    LEAD = RING - 1
    STEPS = timetable(NC, NB)
    PROLOGUE = prologue_steps(NC, NB)

    x_rows = x.rearrange("b t c -> (b t) c")
    out_rows = out.rearrange("b t c -> (b t) c")

    UNIT_CREDIT, HID_CREDIT, ACC_CREDIT, OUT_CREDIT = 1, 2, 2, 1

    with ExitStack() as ctx:
        def sb(name, shape, dtype=FP32):
            return ctx.enter_context(nc.sbuf_tensor(name, shape, dtype))

        def ps(name, shape):
            return ctx.enter_context(nc.psum_tensor(name, shape, FP32))

        def sem(name):
            return ctx.enter_context(nc.semaphore(name))

        w_raw = sb("w_raw", [P, 2, LT, 2 * P])
        w_hi = [sb(f"w_hi{k}", [P, LT, P], FP32R) for k in range(RING)]
        w_lo = [sb(f"w_lo{k}", [P, LT, P], FP32R) for k in range(RING)]
        x_hi = sb("x_hi", [P, NC, K], FP32R)
        x_lo = sb("x_lo", [P, NC, K], FP32R)
        h_hi = sb("h_hi", [P, LT, K], FP32R)
        h_lo = sb("h_lo", [P, LT, K], FP32R)
        h_raw = sb("h_raw", [P, 2, K])
        acc = sb("acc", [P, NC, K])
        x_row = sb("x_row", [P, NB, C])
        tiles_in = sb("tiles_in", [P, 2, NT, P])
        gate = sb("gate", [P, T])
        quad = sb("quad", [P, 4, T])
        sums = sb("sums", [P, 4, T])
        ry = sb("ry", [P, 2, T])
        one_hot = ry[:, :, :].rearrange("p a t -> p (a t)").bitcast(FP16).rearrange("p (t k) -> p t k", k=K)
        even = FrontBuffers(tiles_in[:, 0], tiles_in[:, 1], gate[:, :], quad, sums, ry[:, 0, :], ry[:, 1, :])
        spare = w_raw[:, :, :, :].rearrange("p a (h t) k -> p (a h) (t k)", h=2)
        odd = FrontBuffers(spare[:, 0].rearrange("p (t c) -> p t c", c=P), spare[:, 1].rearrange("p (t c) -> p t c", c=P),
                           spare[:, 2], acc[:, :, :].rearrange("p (a t) k -> p a (t k)", a=4), x_row,
                           spare[:, 3], h_raw[:, :, :].rearrange("p a k -> p (a k)"))

        def buffers(fb, i):
            return odd if isinstance(fb, int) and i % 2 else even

        nf, db = even.nf, even.db
        ident = sb("ident", [P, P])
        before = sb("before", [P, P])
        iota_i = gate[:, 0:K].bitcast(INT32)
        tok_i = gate[:, K:K + NT].bitcast(INT32)
        slot_id = sb("slot_id", [P, K], FP16)
        tok_id = sb("tok_id", [P, NT], FP16)
        wr_row = sb("wr_row", [P, C])
        br_col = sb("br_col", [P, 1])
        NV = 3 * NC + F // P
        cond_all = nf.rearrange("p (b c) -> p b c", b=B)
        vec_rows = db[0:NV, 0:P]
        cols = sb("cols", [P, NV])
        w_col, u_col, b2_col, b1_col = cols[:, 0:NC], cols[:, NC:2 * NC], cols[:, 2 * NC:3 * NC], cols[:, 3 * NC:]
        dec_w = sb("dec_w", [P, NC])
        tf = sb("tf", [P, B])
        dec_f = sb("dec_f", [P, B])
        scale_c = sb("scale_c", [P, B])
        dec = sb("dec", [P, NC])
        scale_now = sb("scale_now", [P, 1])
        parts = sb("parts", [P, NT, NC])
        score = sb("score", [P, 2, NT])
        counts = sb("counts", [P, NT, 3])
        rank = sb("rank", [P, NT])
        row_base = sb("row_base", [P, 1])
        idx_y = sb("idx_y", [P, NB], UINT32)
        idx_next = sb("idx_next", [P, NB], UINT32)
        idx_now = sb("idx_now", [P, NB], UINT32)

        bank = [ps(f"bank{k}", [P, K]) for k in range(2)]
        kT = ps("kT", [P, T])
        denT = ps("denT", [P, T])
        numT = ps("numT", [P, T])
        chosen = numT[:, 0:NB]

        const_loaded = sem("const_loaded")
        const_pool = sem("const_pool")
        const_pe = sem("const_pe")
        const_act = sem("const_act")
        const_dve = sem("const_dve")
        raw_loaded = [sem(f"raw_loaded{k}") for k in range(2)]
        hi_split = sem("hi_split")
        lo_split = sem("lo_split")
        unit_done = sem("unit_done")
        gelu_done = sem("gelu_done")
        hid_hi_done = sem("hid_hi_done")
        hid_done = sem("hid_done")
        acc_done = sem("acc_done")
        kv_loaded = [sem(f"kv_loaded{k}") for k in range(2)]
        x_loaded = [sem(f"x_loaded{k}") for k in range(2)]
        x_copied = [sem(f"x_copied{k}") for k in range(2)]
        keys_done = sem("keys_done")
        exp_done = sem("exp_done")
        seed_step = sem("seed_step")
        seed_weighted = sem("seed_weighted")
        ek_done = sem("ek_done")
        ekv_done = sem("ekv_done")
        gate_done = sem("gate_done")
        eukv_done = sem("eukv_done")
        decay_set = sem("decay_set")
        den_step = sem("den_step")
        den_done = sem("den_done")
        num_step = sem("num_step")
        num_done = sem("num_done")
        denT_done = sem("denT_done")
        numT_done = sem("numT_done")
        rec_step = sem("rec_step")
        y_done = sem("y_done")
        y_stored = [sem(f"y_stored{k}") for k in range(2)]
        yw_done = sem("yw_done")
        part_done = sem("part_done")
        score_step = sem("score_step")
        score_rows_done = sem("score_rows_done")
        count_step = sem("count_step")
        hot_step = sem("hot_step")
        chosen_done = sem("chosen_done")
        idx_step = sem("idx_step")
        idx_copied = sem("idx_copied")
        row_fetched = [sem(f"row_fetched{j}") for j in range(NB)]
        rowT_done = sem("rowT_done")
        x_hi_done = sem("x_hi_done")
        x_split = sem("x_split")
        x_row_loaded = [sem(f"x_row_loaded{j}") for j in range(NB)]
        outT_done = sem("outT_done")
        out_done = sem("out_done")
        scattered = sem("scattered")
        pool_passed = sem("pool_passed")

        def wait(eng, semaphore, count):
            if not (isinstance(count, int) and count <= 0):
                eng.wait_ge(semaphore, count)

        def known(eng, count):
            return count if isinstance(count, int) else eng.snap(count)

        def tiles_free(fb, n):
            return n - 1 if isinstance(fb, int) else n

        def last_here(fb, i):
            if isinstance(fb, int):
                return i % 2, i // 2
            return (i - 1) % 2, NC // 2 * fb + (i + 1) // 2

        RANK_OPS = 3 * NT - 1

        block = ctx.enter_context(nc.Block())

        @block.sync
        def _(sp):
            def met():
                sp.wait_ge(const_loaded, 16 * 7)

            def load_weights(b, pair):
                lot, r = divmod(2 * pair, 2 * LT)
                if r < LT:
                    src = w1[:, lot * LOT + r * P:lot * LOT + (r + 2) * P]
                else:
                    src = w2[lot * LOT:(lot + 1) * LOT, (r - LT) * P:(r - LT + 2) * P]
                wait(sp, lo_split, UNITS * b + 2 * pair - 2)
                sp.dma_start(w_raw[:, pair % 2], src.rearrange("(k p) n -> p k n", p=P)).then_inc(raw_loaded[pair % 2], 16)

            def front_step(step, i, fb):
                n = NC * fb + i
                cs = slice(i * P, (i + 1) * P)
                free = tiles_free(fb, n)
                if step == "load_kv":
                    kv_src = kv_b(fb)[:, :, cs]
                    n = known(sp, free)
                    if not isinstance(fb, int):
                        met()
                    wait(sp, keys_done, n)
                    sp.dma_start(buffers(fb, i).kv_in, kv_src).then_inc(kv_loaded[i % 2], 16)
                elif step == "load_x":
                    x_src = x_b(fb)[:, :, cs]
                    parity, n_copied = last_here(fb, i)
                    n, n_copied = known(sp, free), known(sp, 16 * n_copied)
                    if not isinstance(fb, int):
                        met()
                    wait(sp, gate_done, n)
                    wait(sp, x_copied[parity], n_copied)
                    sp.dma_start(buffers(fb, i).x_in, x_src).then_inc(x_loaded[i % 2], 16)
                elif step == "keep":
                    y_dst = y_rows.rearrange("(t p) c -> p t c", p=P)[:, :, cs]
                    if i == 0:
                        for j in range(NB):
                            wait(sp, row_fetched[j], 16 * fb)
                    met()
                    sp.wait_ge(y_done, n + 1)
                    sp.dma_start(y_dst, buffers(fb, i).y.rearrange("p (t c) -> p t c", c=P)).then_inc(y_stored[i % 2], 16)

            def of_batch(rows, fb):
                start = fb * T if isinstance(fb, int) else sp.snap(fb * T)
                return rows[bass.ds(start, T), :].rearrange("(t p) c -> p t c", p=P)

            def kv_b(fb):
                return of_batch(kv.rearrange("b t c -> (b t) c"), fb)

            def x_b(fb):
                return of_batch(x_rows, fb)

            for step, i in PROLOGUE:
                front_step(step, i, 0)
                if (step, i) == ("load_kv", 0):
                    for k, vec in enumerate((w, u, b2)):
                        sp.dma_start(vec_rows[k * NC:(k + 1) * NC, :], vec.rearrange("(t p) -> t p", p=P)).then_inc(const_loaded, 16)
                    sp.dma_start(vec_rows[3 * NC:NV, :], b1.rearrange("(t p) -> t p", p=P)).then_inc(const_loaded, 16)
                    sp.dma_start(cond_all, cond.partition_broadcast(P)).then_inc(const_loaded, 16)
                    sp.dma_start(wr_row[:], w_r.partition_broadcast(P)).then_inc(const_loaded, 16)
                    sp.dma_start(br_col[:], b_r.partition_broadcast(P)).then_inc(const_loaded, 16)
                if (step, i) == ("keep", NC - 1):
                    sp.wait_ge(keys_done, NC)
                    sp.wait_ge(gate_done, NC)
                    sp.wait_ge(x_copied[1], 16 * (NC // 2))
                    load_weights(0, 0)
                    sp.wait_ge(part_done, NC)
                    load_weights(0, 1)
            load_weights(0, 2)

            def batch(b, front):
                if front:
                    front_step("load_kv", 0, b + 1)
                    front_step("load_x", 0, b + 1)
                for s in range(UNITS):
                    if s % 2 == 0 and (front or s // 2 + 3 < UNITS // 2):
                        pair = s // 2 + 3
                        if pair < UNITS // 2:
                            load_weights(b, pair)
                        else:
                            load_weights(b + 1, pair - UNITS // 2)
                    if front:
                        for step, i in STEPS[s]:
                            front_step(step, i, b + 1)

            with sp.Fori(0, B - 1) as b:
                batch(b, True)
            batch(B - 1, False)
            sp.wait_ge(scattered, 16 * NB * B)
            for k in range(2):
                sp.wait_ge(x_copied[k], 16 * (TILES // 2))
                sp.wait_ge(y_stored[k], 16 * (TILES // 2))

        @block.tensor
        def _(pe):
            pe.sem_inc(unit_done, UNIT_CREDIT)
            pe.sem_inc(outT_done, OUT_CREDIT)
            pe.wait_ge(const_loaded, 16 * 7)
            pe.wait_ge(const_pool, 2)
            nc.tensor.transpose(denT[:, 0:NV], vec_rows, ident[0:NV, 0:NV]).then_inc(const_pe, 1)

            def turn(dst, src, count, ready):
                for k in range(count):
                    last = nc.tensor.transpose(dst[:, k * P:(k + 1) * P], src(k), ident[:])
                last.then_inc(ready, 1)

            def turn_sum(dst, sources, ready):
                for k in range(NT):
                    for a, src in enumerate(sources):
                        last = nc.tensor.matmul(dst[:, k * P:(k + 1) * P], src[:, k * P:(k + 1) * P], ident[:],
                                                start=(a == 0), stop=(a == len(sources) - 1))
                last.then_inc(ready, 1)

            def front_step(step, i, fb):
                n = NC * fb + i
                f = buffers(fb, i)
                if step == "keys":
                    pe.wait_ge(kv_loaded[i % 2], 16 * (NC // 2 * fb + i // 2 + 1))
                    wait(pe, exp_done, 3 * n)
                    if i == 0 and not isinstance(fb, int):
                        pe.wait_ge(out_done, OUT_CREDIT + NB * (fb - 1))
                    turn(kT, lambda k: f.kv_in[:, k, :], NT, keys_done)
                elif step == "den_back":
                    if n == 0:
                        pe.wait_ge(const_dve, 1)
                    wait(pe, rec_step, 3 * n - 2)
                    pe.wait_ge(den_step, 3 * n + 3)
                    turn_sum(denT, (f.df, f.db, f.euk), denT_done)
                elif step == "num_back" and isinstance(fb, int):
                    wait(pe, y_done, n)
                    pe.wait_ge(num_step, 5 * n + 5)
                    pe.wait_ge(eukv_done, n + 1)
                    turn_sum(numT, (f.nf, f.nb, f.v), numT_done)
                elif step == "num_back":
                    pe.wait_ge(num_done, n + 1)
                    turn(numT, lambda k: f.nf[:, k * P:(k + 1) * P], NT, numT_done)
                elif step == "score_rows":
                    pe.wait_ge(score_step, 3 * fb + 3)
                    turn(denT, lambda k: nf[:, k * P:(k + 1) * P], NT, score_rows_done)
                elif step == "choose":
                    pe.wait_ge(hot_step, 9 * fb + 9)
                    for j in range(NB):
                        for t in range(NT):
                            last = nc.tensor.matmul(chosen[:, j:j + 1], one_hot[:, t, j * P:(j + 1) * P],
                                                    tok_id[:, t:t + 1], start=(t == 0), stop=(t == NT - 1))
                    last.then_inc(chosen_done, 1)
                elif step == "take_rows":
                    pe.wait_ge(row_fetched[i], 16 * (fb + 1))
                    if i == 0:
                        pe.wait_ge(exp_done, 3 * NC * (fb + 1))
                    elif i == 1:
                        pe.wait_ge(idx_step, 3 * fb + 2)
                    elif i == 2:
                        pe.wait_ge(count_step, RANK_OPS * (fb + 1))
                    else:
                        pe.wait_ge(x_split, NB * fb + 1)
                    turn((kT, numT, denT, kT)[i], lambda k: quad[:, i, k * P:(k + 1) * P], NC, rowT_done)

            for step, i in PROLOGUE:
                front_step(step, i, 0)

            def unit(b, s):
                lot, r = divmod(s, 2 * LT)
                hidden = LT * (F // LOT) * b + LT * lot
                k_hi, k_lo = w_hi[s % RING], w_lo[s % RING]
                if r < 2:
                    pe.wait_ge(acc_done, ACC_CREDIT + hidden - 1 + r)
                elif r < LT + 2:
                    pe.wait_ge(gelu_done, hidden + r - 1)
                else:
                    pe.wait_ge(acc_done, ACC_CREDIT + hidden + r - LT - 1)
                if s == 0:
                    pe.wait_ge(x_split, NB * (b + 1))
                pe.wait_ge(lo_split, UNITS * b + s + 1)
                m_hi, m_lo = (x_hi, x_lo) if r < LT else (h_hi, h_lo)
                for k in range(LT):
                    if r == LT:
                        pe.wait_ge(hid_done, HID_CREDIT + hidden + k + 1)
                    nc.tensor.matmul(bank[s % 2][:], k_hi[:, k, :], m_hi[:, k, :], start=(k == 0), stop=False)
                    nc.tensor.matmul(bank[s % 2][:], k_hi[:, k, :], m_lo[:, k, :], start=False, stop=False)
                    last = nc.tensor.matmul(bank[s % 2][:], k_lo[:, k, :], m_hi[:, k, :], start=False, stop=(k == LT - 1))
                last.then_inc(unit_done, 1)

            def output_back(b, front):
                pe.wait_ge(acc_done, ACC_CREDIT + LT * (F // LOT) * (b + 1))
                if front:
                    pe.wait_ge(x_split, NB * (b + 2))
                for j in range(NB):
                    if j == 3:
                        pe.wait_ge(out_done, OUT_CREDIT + NB * b + 1)
                    turn((denT, kT, numT, denT)[j], lambda k: acc[:, k, j * P:(j + 1) * P], NC, outT_done)

            def batch(b, front):
                for s in range(UNITS):
                    unit(b, s)
                    if front:
                        for step, i in STEPS[s]:
                            front_step(step, i, b + 1)
                output_back(b, front)

            with pe.Fori(0, B - 1) as b:
                batch(b, True)
            batch(B - 1, False)

        @block.scalar
        def _(act):
            act.wait_ge(const_dve, 1)
            nc.scalar.activation(dec_w[:], w_col, ACT.Exp).then_inc(const_act, 1)
            act.wait_ge(const_act, 1)
            nc.scalar.activation(dec_w[:], dec_w[:], ACT.Exp, scale=-1.0).then_inc(const_act, 1)
            act.wait_ge(const_dve, 2)
            nc.scalar.activation(tf[:], tf[:], ACT.Exp, scale=-1.0).then_inc(const_act, 1)

            def split_hi(b, s):
                pair = s // 2
                wait(act, unit_done, UNIT_CREDIT + UNITS * b + s - LEAD)
                act.wait_ge(raw_loaded[pair % 2], 16 * (UNITS // 4 * b + pair // 2 + 1))
                nc.scalar.activation(w_hi[s % RING][:], w_raw[:, pair % 2, :, (s % 2) * P:(s % 2 + 1) * P],
                                     ACT.Copy).then_inc(hi_split, 1)

            def front_step(step, i, fb):
                n = NC * fb + i
                f = buffers(fb, i)
                if step == "weigh":
                    act.wait_ge(keys_done, n + 1)
                    if isinstance(fb, int):
                        wait(act, numT_done, n - 1)
                    else:
                        act.wait_ge(num_done, n)
                    if i == 0:
                        wait(act, rowT_done, NB * fb)
                    nc.scalar.activation(f.ek, kT[:], ACT.Exp).then_inc(exp_done, 1)
                    nc.scalar.activation(f.v, kT[:], ACT.Copy).then_inc(exp_done, 1)
                    nc.scalar.activation(f.euk, kT[:], ACT.Exp, bias=u_col[:, i:i + 1]).then_inc(exp_done, 1)
                    x_dst = out_rows[bass.ds(fb * T, T), i * P:(i + 1) * P].rearrange("(t p) c -> p t c", p=P)
                    act.wait_ge(x_loaded[i % 2], 16 * (NC // 2 * fb + i // 2 + 1))
                    act.dma_start(x_dst, f.x_in).then_inc(x_copied[i % 2], 16)
                elif step == "gate":
                    act.wait_ge(x_loaded[i % 2], 16 * (NC // 2 * fb + i // 2 + 1))
                    if isinstance(fb, int):
                        wait(act, rec_step, 3 * (n - 1))
                    else:
                        act.wait_ge(y_done, n)
                    if isinstance(n, int) and n == 0:
                        act.wait_ge(const_dve, 14)
                    nc.scalar.activation(f.gate, f.x_in.rearrange("p t c -> p (t c)"), ACT.Sigmoid).then_inc(gate_done, 1)
                elif step == "seed":
                    act.wait_ge(rec_step, 3 * n + 1)
                    nc.scalar.activation(f.df, f.rec, ACT.Ln).then_inc(seed_step, 1)
                    act.wait_ge(seed_step, 2 * n + 1)
                    nc.scalar.activation(f.df, f.df, ACT.Exp, scale=-1.0).then_inc(seed_step, 1)
                elif step == "take_rows":
                    act.wait_ge(rowT_done, NB * fb + i + 1)
                    src = (kT, numT, denT, kT)[i]
                    nc.scalar.activation(x_hi[:, :, i * P:(i + 1) * P], src[:].rearrange("p (c r) -> p c r", r=P),
                                         ACT.Copy).then_inc(x_hi_done, 1)

            for step, i in PROLOGUE:
                front_step(step, i, 0)
                if step == "score":
                    split_hi(0, 0)
                    split_hi(0, 1)
                elif step == "one_hot":
                    split_hi(0, 2)

            def batch(b, front):
                for s in range(UNITS):
                    lot, r = divmod(s, 2 * LT)
                    if s + LEAD < UNITS:
                        split_hi(b, s + LEAD)
                    elif front:
                        split_hi(b + 1, s + LEAD - UNITS)
                    if r < LT:
                        m = LT * (F // LOT) * b + LT * lot + r
                        act.wait_ge(unit_done, UNIT_CREDIT + UNITS * b + s + 1)
                        act.wait_ge(hid_done, HID_CREDIT + m - 1)
                        nc.scalar.activation(h_raw[:, r % 2, :], bank[s % 2][:], ACT.Gelu_apprx_tanh,
                                             bias=b1_col[:, LT * lot + r:LT * lot + r + 1]).then_inc(gelu_done, 1)
                    if front:
                        for step, i in STEPS[s]:
                            front_step(step, i, b + 1)

            with act.Fori(0, B - 1) as b:
                batch(b, True)
            batch(B - 1, False)

        @block.vector
        def _(dve):
            dve.sem_inc(hid_done, HID_CREDIT)
            dve.sem_inc(acc_done, ACC_CREDIT)
            dve.sem_inc(out_done, OUT_CREDIT)
            dve.wait_ge(const_pe, 1)
            nc.vector.tensor_copy(cols[:], denT[:, 0:NV]).then_inc(const_dve, 1)
            nc.vector.tensor_reduce(tf[:], cond_all, AXIS_X, ALU.add).then_inc(const_dve, 1)
            dve.wait_ge(const_act, 3)
            nc.vector.tensor_scalar(tf[:], tf[:], 1.0, None, ALU.add).then_inc(const_dve, 1)
            dve.wait_ge(const_dve, 3)
            nc.vector.reciprocal(tf[:], tf[:]).then_inc(const_dve, 1)
            dve.wait_ge(const_dve, 4)
            nc.vector.tensor_scalar(dec_f[:], tf[:], 0.5, 0.5, ALU.mult, ALU.add).then_inc(const_dve, 1)
            nc.vector.tensor_scalar(scale_c[:], tf[:], 0.2, 0.8, ALU.mult, ALU.add).then_inc(const_dve, 1)
            for f in (even, odd):
                nc.vector.memset(f.db[:, T - 1:T], 0.0).then_inc(const_dve, 1)
                nc.vector.memset(f.nb[:, T - 1:T], 0.0).then_inc(const_dve, 1)
            nc.vector.memset(counts[:], 0.0).then_inc(const_dve, 1)
            nc.vector.memset(row_base[:], 0.0).then_inc(const_dve, 1)
            dve.wait_ge(const_pool, 5)
            nc.vector.tensor_copy(slot_id[:], iota_i).then_inc(const_dve, 1)
            nc.vector.tensor_copy(tok_id[:], tok_i).then_inc(const_dve, 1)
            dve.wait_ge(const_dve, 14)

            def count(out, in0, scalar, op, t):
                nc.vector.tensor_scalar(out, in0, scalar, 0.0, op, ALU.add, accum_out=t).then_inc(count_step, 1)

            def rank_tiles(fb, tiles):
                for t in tiles:
                    col = score[:, 1, t:t + 1]
                    unread = (even.df, even.nf, even.ek, even.euk)[t % 4]
                    if t >= 4:
                        dve.wait_ge(count_step, RANK_OPS * fb + 3 * (t - 3) - 1)
                    if t:
                        count(unread[:, 0:t * P], denT[:, 0:t * P], col, ALU.is_ge, counts[:, t, 0:1])
                    count(unread[:, t * P:T], denT[:, t * P:T], col, ALU.is_gt, counts[:, t, 1:2])
                    nc.vector.scalar_tensor_tensor(
                        even.ekv[:, t * P:(t + 1) * P], denT[:, t * P:(t + 1) * P], col, before[:],
                        ALU.is_equal, ALU.mult, accum_out=counts[:, t, 2:3]).then_inc(count_step, 1)

            def front_step(step, i, fb):
                n = NC * fb + i
                f = buffers(fb, i)
                free = tiles_free(fb, n)
                if step == "clamp":
                    dve.wait_ge(exp_done, 3 * n + 1)
                    nc.vector.tensor_scalar(f.ek, f.ek, E30, None, ALU.min).then_inc(ek_done, 1)
                elif step == "den_scans":
                    if i == 0:
                        nc.vector.tensor_scalar(dec[:], dec_w[:], dec_f[:, bass.ds(fb, 1)], None,
                                                ALU.mult).then_inc(decay_set, 1)
                        sign = -1.0 if isinstance(fb, int) else 1.0
                        nc.vector.tensor_scalar(scale_now[:], scale_c[:, bass.ds(fb, 1)], sign, None,
                                                ALU.mult).then_inc(decay_set, 1)
                    decay = dec[:, i:i + 1].to_broadcast([P, T])
                    dve.wait_ge(decay_set, 2 * fb + 2)
                    dve.wait_ge(ek_done, n + 1)
                    if isinstance(fb, int):
                        wait(dve, y_done, free)
                    nc.vector.tensor_tensor_scan(f.df, decay, f.ek, 0.0, ALU.mult, ALU.add).then_inc(den_step, 1)
                    nc.vector.tensor_tensor_scan(f.db[:, T - 2::-1], f.ek[:, T - 1:0:-1], decay[:, 0:T - 1], 0.0,
                                                 ALU.add, ALU.mult).then_inc(den_step, 1)
                    dve.wait_ge(exp_done, 3 * n + 3)
                    if isinstance(fb, int):
                        nc.vector.tensor_scalar(f.euk, f.euk, E30, None, ALU.min).then_inc(den_step, 1)
                    else:
                        dve.wait_ge(den_step, 3 * n + 1)
                        nc.vector.scalar_tensor_tensor(f.df, f.euk, E30, f.df, ALU.min, ALU.add).then_inc(den_step, 1)
                elif step == "den_sum":
                    dve.wait_ge(den_step, 3 * n + 3)
                    nc.vector.tensor_tensor(f.df, f.df, f.db, ALU.add).then_inc(den_done, 1)
                    dve.wait_ge(den_done, n + 1)
                    nc.vector.tensor_scalar(f.df, f.df, DEN_FLOOR, None, ALU.max).then_inc(rec_step, 1)
                elif step == "num_scans":
                    decay = dec[:, i:i + 1].to_broadcast([P, T])
                    dve.wait_ge(ekv_done, n + 1)
                    wait(dve, numT_done, free)
                    nc.vector.tensor_tensor_scan(f.nf, decay, f.ekv, 0.0, ALU.mult, ALU.add).then_inc(num_step, 1)
                    nc.vector.tensor_tensor_scan(f.nb[:, T - 2::-1], f.ekv[:, T - 1:0:-1], decay[:, 0:T - 1], 0.0,
                                                 ALU.add, ALU.mult).then_inc(num_step, 4 if isinstance(fb, int) else 1)
                elif step == "own_part":
                    nc.vector.scalar_tensor_tensor(f.euk, f.euk, E30, f.v, ALU.min, ALU.mult).then_inc(num_step, 1)
                elif step == "num_sum":
                    dve.wait_ge(num_step, 5 * n + 2)
                    nc.vector.tensor_tensor(f.nf, f.nf, f.nb, ALU.add).then_inc(num_step, 1)
                elif step == "quotient":
                    dve.wait_ge(num_step, 5 * n + 4)
                    nc.vector.tensor_tensor(f.nf, f.nf, f.euk, ALU.add).then_inc(num_step, 1)
                    dve.wait_ge(rec_step, 3 * n + 3)
                    dve.wait_ge(num_step, 5 * n + 5)
                    nc.vector.tensor_tensor(f.nf, f.nf, f.df, ALU.mult).then_inc(num_done, 1)
                elif step == "divide_a" and isinstance(fb, int):
                    dve.wait_ge(denT_done, n + 1)
                    wait(dve, part_done, free)
                    nc.vector.tensor_scalar(f.rec, denT[:], DEN_FLOOR, None, ALU.max).then_inc(rec_step, 1)
                elif step == "divide_b" and isinstance(fb, int):
                    dve.wait_ge(seed_step, 2 * n + 2)
                    nc.vector.tensor_tensor(f.rec, f.rec, f.df, ALU.mult).then_inc(rec_step, 1)
                    dve.wait_ge(rec_step, 3 * n + 2)
                    dve.wait_ge(seed_weighted, n + 1)
                    nc.vector.scalar_tensor_tensor(f.rec, f.rec, 2.0, f.gate, ALU.subtract, ALU.mult).then_inc(rec_step, 1)
                elif step == "divide_a":
                    dve.wait_ge(rec_step, 3 * n + 1)
                    nc.vector.reciprocal(f.df[:, 0:T // 2], f.df[:, 0:T // 2]).then_inc(rec_step, 1)
                elif step == "divide_b":
                    nc.vector.reciprocal(f.df[:, T // 2:], f.df[:, T // 2:]).then_inc(rec_step, 1)
                elif step == "weight":
                    dve.wait_ge(numT_done, n + 1)
                    parity, n_stored = last_here(fb, i)
                    wait(dve, y_stored[parity], 16 * n_stored)
                    wait(dve, yw_done, free)
                    if isinstance(fb, int):
                        dve.wait_ge(rec_step, 3 * n + 3)
                        weights = f.rec
                    else:
                        dve.wait_ge(gate_done, n + 1)
                        wait(dve, part_done, n)
                        weights = f.gate
                        if i == 0:
                            dve.wait_ge(chosen_done, fb)
                    nc.vector.scalar_tensor_tensor(f.y, numT[:], scale_now[:, 0:1], weights, ALU.mult,
                                                   ALU.mult).then_inc(y_done, 1)
                elif step == "score_part":
                    dve.wait_ge(yw_done, n + 1)
                    nc.vector.tensor_reduce(parts[:, :, i], f.rec.rearrange("p (t c) -> p t c", c=P), AXIS_X,
                                            ALU.add).then_inc(part_done, 1)
                elif step == "score":
                    dve.wait_ge(part_done, NC * (fb + 1))
                    nc.vector.tensor_reduce(score[:, 0, :], parts[:], AXIS_X, ALU.add).then_inc(score_step, 1)
                    dve.wait_ge(score_step, 3 * fb + 1)
                    nc.vector.tensor_scalar(score[:, 1, :], score[:, 0, :], br_col[:, 0:1], None,
                                            ALU.add).then_inc(score_step, 1)
                    dve.wait_ge(score_step, 3 * fb + 2)
                    dve.wait_ge(numT_done, NC * (fb + 1))
                    nc.vector.tensor_copy(nf[:].rearrange("p (t c) -> p t c", c=P),
                                          score[:, 1, :].unsqueeze(2).to_broadcast([P, NT, P])).then_inc(score_step, 1)
                elif step == "rank_a":
                    dve.wait_ge(score_rows_done, fb + 1)
                    rank_tiles(fb, range(0, NT // 2))
                elif step == "rank_b":
                    rank_tiles(fb, range(NT // 2, NT))
                elif step == "one_hot":
                    dve.wait_ge(count_step, RANK_OPS * (fb + 1))
                    nc.vector.tensor_reduce(rank[:], counts[:], AXIS_X, ALU.add).then_inc(hot_step, 1)
                    dve.wait_ge(hot_step, 9 * fb + 1)
                    for k in range(2):
                        dve.wait_ge(y_stored[k], 16 * (NC // 2) * (fb + 1))
                    for t in range(NT):
                        nc.vector.tensor_scalar(one_hot[:, t, :], slot_id[:], rank[:, t:t + 1], None,
                                                ALU.is_equal).then_inc(hot_step, 1)
                elif step == "choose":
                    dve.wait_ge(chosen_done, fb + 1)
                    wait(dve, idx_copied, fb)
                    nc.vector.tensor_copy(idx_y[:], chosen).then_inc(idx_step, 1)
                    nc.vector.tensor_scalar(idx_next[:], chosen, row_base[:, 0:1], None, ALU.add).then_inc(idx_step, 1)
                    dve.wait_ge(idx_step, 3 * fb + 2)
                    nc.vector.tensor_scalar(row_base[:], row_base[:], float(T), None, ALU.add).then_inc(idx_step, 1)
                elif step == "take_rows":
                    dve.wait_ge(x_hi_done, NB * fb + i + 1)
                    src = (kT, numT, denT, kT)[i]
                    rows = slice(i * P, (i + 1) * P)
                    nc.vector.tensor_tensor(x_lo[:, :, rows], src[:].rearrange("p (c r) -> p c r", r=P),
                                            x_hi[:, :, rows].bitcast(FP32), ALU.subtract).then_inc(x_split, 1)

            for step, i in PROLOGUE:
                front_step(step, i, 0)
            dve.sem_inc(den_done, NC)
            dve.sem_inc(num_done, NC)

            def batch(b, front):
                for s in range(UNITS):
                    lot, r = divmod(s, 2 * LT)
                    if r < LT:
                        m = LT * (F // LOT) * b + LT * lot + r
                        dve.wait_ge(gelu_done, m + 1)
                        nc.vector.tensor_copy(h_hi[:, r, :], h_raw[:, r % 2, :]).then_inc(hid_hi_done, 1)
                        dve.wait_ge(hid_hi_done, m + 1)
                        nc.vector.tensor_tensor(h_lo[:, r, :], h_raw[:, r % 2, :], h_hi[:, r, :].bitcast(FP32),
                                                ALU.subtract).then_inc(hid_done, 1)
                    else:
                        dve.wait_ge(unit_done, UNIT_CREDIT + UNITS * b + s + 1)
                        if lot == 0:
                            if r == LT:
                                dve.wait_ge(outT_done, OUT_CREDIT + NB * b)
                            nc.vector.tensor_scalar(acc[:, r - LT, :], bank[s % 2][:], b2_col[:, r - LT:r - LT + 1], None,
                                                    ALU.add).then_inc(acc_done, 1)
                        else:
                            nc.vector.tensor_tensor(acc[:, r - LT, :], acc[:, r - LT, :], bank[s % 2][:],
                                                    ALU.add).then_inc(acc_done, 1)
                    if front:
                        for step, i in STEPS[s]:
                            front_step(step, i, b + 1)
                for j in range(NB):
                    dve.wait_ge(outT_done, OUT_CREDIT + NB * b + j + 1)
                    dve.wait_ge(x_row_loaded[j], 16 * (b + 1))
                    nc.vector.tensor_tensor(x_row[:, j, :], (denT, kT, numT, denT)[j][:], x_row[:, j, :],
                                            ALU.add).then_inc(out_done, 1)

            with dve.Fori(0, B - 1) as b:
                batch(b, True)
            batch(B - 1, False)

        @block.gpsimd
        def _(pool):
            nc.gpsimd.memset(ident[:], 0.0).then_inc(const_pool, 1)
            pool.wait_ge(const_pool, 1)
            nc.gpsimd.affine_select(out=ident[:], in_=ident[:], compare_op=ALU.not_equal, fill=1.0, base=0,
                                    pattern=[[-1, P]], channel_multiplier=1).then_inc(const_pool, 1)
            nc.gpsimd.memset(before[:], 1.0).then_inc(const_pool, 1)
            nc.gpsimd.iota(iota_i, pattern=[[1, K]], base=0, channel_multiplier=0).then_inc(const_pool, 1)
            nc.gpsimd.iota(tok_i, pattern=[[P, NT]], base=0, channel_multiplier=1).then_inc(const_pool, 1)
            pool.wait_ge(const_pool, 3)
            nc.gpsimd.affine_select(out=before[:], in_=before[:], compare_op=ALU.is_gt, fill=0.0, base=0,
                                    pattern=[[-1, P]], channel_multiplier=1).then_inc(const_pool, 1)

            def passed():
                pool.sem_inc(pool_passed, 1)

            def split_lo(b, s):
                pair = s // 2
                pool.wait_ge(hi_split, UNITS * b + s + 1)
                nc.gpsimd.tensor_tensor(w_lo[s % RING][:], w_raw[:, pair % 2, :, (s % 2) * P:(s % 2 + 1) * P],
                                        w_hi[s % RING][:].bitcast(FP32), ALU.subtract).then_inc(lo_split, 1)

            def front_step(step, i, fb):
                n = NC * fb + i
                f = buffers(fb, i)
                if step == "clamp":
                    pool.wait_ge(ek_done, n + 1)
                    pool.wait_ge(exp_done, 3 * n + 2)
                    nc.gpsimd.tensor_tensor(f.ekv, f.ek, f.v, ALU.mult).then_inc(ekv_done, 1)
                elif step == "den_scans" and isinstance(fb, int):
                    pool.wait_ge(den_step, 3 * n + 3)
                    pool.wait_ge(ekv_done, n + 1)
                    nc.gpsimd.tensor_tensor(f.v, f.v, f.euk, ALU.mult).then_inc(eukv_done, 1)
                elif step == "seed":
                    pool.wait_ge(seed_step, 2 * n + 2)
                    pool.wait_ge(gate_done, n + 1)
                    nc.gpsimd.tensor_tensor(f.gate, f.gate, f.df, ALU.mult).then_inc(seed_weighted, 1)
                elif step == "keep":
                    pool.wait_ge(y_done, n + 1)
                    nc.gpsimd.tensor_tensor(f.rec.rearrange("p (t c) -> p t c", c=P), f.y.rearrange("p (t c) -> p t c", c=P),
                                            wr_row[:, i * P:(i + 1) * P].unsqueeze(1).to_broadcast([P, NT, P]),
                                            ALU.mult).then_inc(yw_done, 1)
                elif step == "fetch":
                    pool.wait_ge(idx_step, 3 * fb + 2)
                    for k in range(2):
                        pool.wait_ge(y_stored[k], 16 * (NC // 2) * (fb + 1))
                    pool.wait_ge(numT_done, NC * (fb + 1))
                    passed()
                    for j in range(NB):
                        nc.gpsimd.indirect_dma_start(
                            out=quad[:, j, :], out_offset=None, in_=y_rows,
                            in_offset=bass.IndirectOffsetOnAxis(ap=idx_y[:, j:j + 1], axis=0),
                        ).then_inc(row_fetched[j], 16)

            def fetch_x_rows(fb):
                wait(pool, scattered, 16 * NB * fb)
                pool.wait_ge(idx_step, 3 * fb + 2)
                passed()
                nc.gpsimd.tensor_copy(idx_now[:], idx_next[:]).then_inc(idx_copied, 1)
                pool.wait_ge(idx_copied, fb + 1)
                passed()
                for j in range(NB):
                    nc.gpsimd.indirect_dma_start(
                        out=x_row[:, j, :], out_offset=None, in_=x_rows,
                        in_offset=bass.IndirectOffsetOnAxis(ap=idx_now[:, j:j + 1], axis=0),
                    ).then_inc(x_row_loaded[j], 16)

            def store_rows(b):
                for j in range(NB):
                    pool.wait_ge(out_done, OUT_CREDIT + NB * b + j + 1)
                    for k in range(2):
                        pool.wait_ge(x_copied[k], 16 * (NC // 2) * (b + 1))
                    passed()
                    nc.gpsimd.indirect_dma_start(
                        out=out_rows, out_offset=bass.IndirectOffsetOnAxis(ap=idx_now[:, j:j + 1], axis=0),
                        in_=x_row[:, j, :], in_offset=None,
                    ).then_inc(scattered, 16)

            pool.wait_ge(const_dve, 1)
            pool.wait_ge(const_dve, 14)
            for step, i in PROLOGUE:
                front_step(step, i, 0)
                if step == "score":
                    split_lo(0, 0)
                    split_lo(0, 1)
                elif step == "one_hot":
                    split_lo(0, 2)

            def batch(b, front):
                for s in range(UNITS):
                    if s + LEAD < UNITS:
                        split_lo(b, s + LEAD)
                    elif front:
                        split_lo(b + 1, s + LEAD - UNITS)
                    if s == 20:
                        fetch_x_rows(b)
                    if front:
                        for step, i in STEPS[s]:
                            front_step(step, i, b + 1)
                store_rows(b)

            with pool.Fori(0, B - 1) as b:
                batch(b, True)
            batch(B - 1, False)


_INS = ["x", "fside_BxSxS_0", "cond_512", "L0_cond_w", "L0_cond_u", "L0_ffn_w_r", "L0_ffn_b_r",
        "L0_ffn_w1", "L0_ffn_b1", "L0_ffn_w2", "L0_ffn_b2"]


def kernel(**inputs):
    import numpy as _np
    import concourse.bacc as _bacc
    from concourse import mybir as _mybir
    from concourse.bass_utils import run_bass_kernel_spmd as _run

    nc = _bacc.Bacc("TRN2", target_bir_lowering=False, num_devices=1, dynamic_dma_scratch_size=4096)
    arrays, args = {}, []
    for name in _INS:
        a = _np.ascontiguousarray(inputs[name])
        if a.ndim == 0:
            a = a.reshape(1)
        arrays[f"in_{name}"] = a
        args.append(nc.dram_tensor(f"in_{name}", a.shape, _mybir.dt.from_np(a.dtype), kind="ExternalInput").ap())
    B, T, C = arrays["in_x"].shape
    y_rows = nc.dram_tensor("y_rows", (T, C), _mybir.dt.float32).ap()
    out = nc.dram_tensor("out_x", (B, T, C), _mybir.dt.float32, kind="ExternalOutput").ap()
    wkv_ffn(nc, *args, y_rows, out)
    r = _run(nc, [arrays], core_ids=[0])
    return r.results[0]["out_x"]
```
